# Optimizing a Trainium2 kernel written in Bass

```python
import numpy as np
import jax
import jax.numpy as jnp

def _softmax(x, axis=-1):
    return jax.nn.softmax(x, axis=axis)

def _gelu(x):
    return jax.nn.gelu(x, approximate=True)

def _silu(x):
    return jax.nn.silu(x)

def _sigmoid(x):
    return jax.nn.sigmoid(x)

def _layernorm(x, axis=-1, eps=1e-05):
    m = jnp.mean(x, axis=axis, keepdims=True)
    v = jnp.var(x, axis=axis, keepdims=True)
    return (x - m) / jnp.sqrt(v + eps)

def _scatter_add(tgt, idx, src, axis=0):
    return tgt.at[idx].add(src)

def _segment_sum(src, seg, n):
    return jax.ops.segment_sum(src, seg, n)
kernel_name = 'mk_xattn_seq_d1_seqx_r2_0bd140'

def setup_inputs(seed: int=0):
    np.random.seed(seed)
    _w = jnp.asarray

    def _rec_inputs():
        import jax
        import jax.numpy as jnp
        _rk = jax.random.key(seed)
        x = -0.0005207 + 1.001 * jax.random.normal(jax.random.fold_in(_rk, 1), (16, 512, 512), jnp.float32)
        _lenS = 512 - jax.random.randint(jax.random.fold_in(_rk, 7), (16,), 0, max(1, 512 // 4) + 1, jnp.int32)
        _lenS2 = 512 - jax.random.randint(jax.random.fold_in(_rk, 8), (16,), 0, max(1, 512 // 4) + 1, jnp.int32)
        _ctx_1024P = jax.random.normal(jax.random.fold_in(_rk, 11), (16, 16, 512), jnp.float32)
        _ctx_1024c = jax.random.dirichlet(jax.random.fold_in(_rk, 511), 0.3 * jnp.ones((16,), jnp.float32), (16, 512))
        _ctx_1024t = jnp.einsum('bsk,bkd->bsd', _ctx_1024c, _ctx_1024P)
        _ctx_1024t = _ctx_1024t * jax.lax.rsqrt(jnp.mean(jnp.square(_ctx_1024t)) + 1e-12) * 0.953939
        ctx_1024 = -1.39393e-06 + 0.999914 * (_ctx_1024t + 0.3 * jax.random.normal(jax.random.fold_in(_rk, 611), (16, 512, 512), jnp.float32))
        _validS = jnp.arange(512)[None, :] < _lenS[:, None]
        _validS2 = jnp.arange(512)[None, :] < _lenS2[:, None]
        _causal = jnp.tril(jnp.ones((512, 512), dtype=bool))
        mask_BxSxS2_ik1 = jnp.where(jnp.broadcast_to(_validS2[:, None, :], (16, 512, 512)), 1, 0).astype(jnp.int32)
        return (x, ctx_1024, mask_BxSxS2_ik1)
    x, ctx_1024, mask_BxSxS2_ik1 = _rec_inputs()

    def _L0_xattn_setup():
        import jax, jax.numpy as jnp
        import numpy as np
        H = 512
        NH = 16
        HD = H // NH
        EPS = 1e-05

        def _split_heads(x, B, L):
            return x.reshape(B, L, NH, HD).transpose(0, 2, 1, 3)
        key = jax.random.key(seed)
        ks = jax.random.split(key, 16)
        B, LQ, LK = (2, 512, 1024)
        s = 1.0 / np.sqrt(H)
        inp = {'query': jax.random.normal(ks[0], (B, LQ, H), jnp.float32), 'key': jax.random.normal(ks[1], (B, LK, H), jnp.float32), 'value': jax.random.normal(ks[2], (B, LK, H), jnp.float32), 'mask': jax.random.randint(ks[3], (B, LQ, LK), 0, 2, jnp.int32), 'Wq': jax.random.normal(ks[4], (H, H), jnp.float32) * s, 'bq': jnp.zeros((H,), jnp.float32), 'Wk': jax.random.normal(ks[5], (H, H), jnp.float32) * s, 'bk': jnp.zeros((H,), jnp.float32), 'Wv': jax.random.normal(ks[6], (H, H), jnp.float32) * s, 'bv': jnp.zeros((H,), jnp.float32), 'Wo': jax.random.normal(ks[7], (H, H), jnp.float32) * s, 'bo': jnp.zeros((H,), jnp.float32), 'ln_g': jnp.ones((H,), jnp.float32), 'ln_b': jnp.zeros((H,), jnp.float32)}
        return inp
    _L0_xattn_all = _L0_xattn_setup()
    _L0_xattn_in = {k: v for k, v in _L0_xattn_all.items() if k in ('Wq', 'bq', 'Wk', 'bk', 'Wv', 'bv', 'Wo', 'bo', 'ln_g', 'ln_b')}
    del _L0_xattn_all
    return {'x': x, 'ctx_1024': ctx_1024, 'mask_BxSxS2_ik1': mask_BxSxS2_ik1, 'L0_xattn_Wq': _L0_xattn_in['Wq'], 'L0_xattn_bq': _L0_xattn_in['bq'], 'L0_xattn_Wk': _L0_xattn_in['Wk'], 'L0_xattn_bk': _L0_xattn_in['bk'], 'L0_xattn_Wv': _L0_xattn_in['Wv'], 'L0_xattn_bv': _L0_xattn_in['bv'], 'L0_xattn_Wo': _L0_xattn_in['Wo'], 'L0_xattn_bo': _L0_xattn_in['bo'], 'L0_xattn_ln_g': _L0_xattn_in['ln_g'], 'L0_xattn_ln_b': _L0_xattn_in['ln_b']}

def reference(x, ctx_1024, mask_BxSxS2_ik1, L0_xattn_Wq, L0_xattn_bq, L0_xattn_Wk, L0_xattn_bk, L0_xattn_Wv, L0_xattn_bv, L0_xattn_Wo, L0_xattn_bo, L0_xattn_ln_g, L0_xattn_ln_b):
    import jax
    import jax.numpy as jnp

    def _L0_xattn_ref(query, key, value, mask, Wq, bq, Wk, bk, Wv, bv, Wo, bo, ln_g, ln_b):
        import jax, jax.numpy as jnp
        import numpy as np
        H = 512
        NH = 16
        HD = H // NH
        EPS = 1e-05

        def _split_heads(x, B, L):
            return x.reshape(B, L, NH, HD).transpose(0, 2, 1, 3)
        B, LQ, _ = query.shape
        LK = key.shape[1]
        Q = _split_heads(query @ Wq.T + bq, B, LQ)
        K = _split_heads(key @ Wk.T + bk, B, LK)
        V = _split_heads(value @ Wv.T + bv, B, LK)
        scores = jnp.einsum('bhqd,bhkd->bhqk', Q, K) / np.sqrt(HD)
        scores = jnp.where(mask[:, None, :, :] == 0, jnp.float32(-1000000000.0), scores)
        attn = jax.nn.softmax(scores, axis=-1)
        ctx = jnp.einsum('bhqk,bhkd->bhqd', attn, V)
        ctx = ctx.transpose(0, 2, 1, 3).reshape(B, LQ, H)
        out = ctx @ Wo.T + bo
        x = out + query
        mu = jnp.mean(x, axis=-1, keepdims=True)
        var = jnp.mean(jnp.square(x - mu), axis=-1, keepdims=True)
        return (x - mu) / jnp.sqrt(var + EPS) * ln_g + ln_b
    x = _L0_xattn_ref(x, ctx_1024, ctx_1024, mask_BxSxS2_ik1, L0_xattn_Wq, L0_xattn_bq, L0_xattn_Wk, L0_xattn_bk, L0_xattn_Wv, L0_xattn_bv, L0_xattn_Wo, L0_xattn_bo, L0_xattn_ln_g, L0_xattn_ln_b)
    return x

_drawn_inputs = setup_inputs


def setup_inputs(seed=0):
    import zlib

    import numpy as np

    out = dict(_drawn_inputs(seed))
    spreads = {'L0_xattn_bq': (0.0, 0.435),
     'L0_xattn_bk': (0.0, 0.8),
     'L0_xattn_bv': (0.0, 0.1),
     'L0_xattn_bo': (0.0, 0.1),
     'L0_xattn_ln_g': (1.0, 0.2),
     'L0_xattn_ln_b': (0.0, 0.1)}
    factors = {}
    for name, (base, spread) in spreads.items():
        noise = np.random.default_rng([zlib.crc32(name.encode()), seed]).standard_normal(out[name].shape)
        drawn = base * np.exp(spread * noise) if base else spread * noise
        out[name] = jnp.asarray(drawn.astype(out[name].dtype))
    for name, factor in factors.items():
        out[name] = (out[name] * factor).astype(out[name].dtype)
    return out
```

```python
from contextlib import ExitStack

import concourse.bass as bass
from concourse import mybir

FP32 = mybir.dt.float32
FP32R = mybir.dt.float32r
BF16 = mybir.dt.bfloat16
INT32 = mybir.dt.int32
ALU = mybir.AluOpType
ACT = mybir.ActivationFunctionType
AX = mybir.AxisListType

NB = 16
L = 512
H = 512
P = 128
NH = 16
D = H // NH
HG = P // D
NG = NH // HG
NC = L // P
NK = H // P
EPS = 1e-5
SCALE = float(D) ** -0.5
MASKED = -1.0e9

BPS = NG * NC
SPS = BPS * HG
STEPS = NB * SPS
LEAD = 3
CHUNKS_AT = ((), (0,), (1,), (2, 3))
SEQS_PER_TURN = 2
TURN = SEQS_PER_TURN * SPS
START = -10 * HG
END = STEPS + 6 * HG
FULL = 16


class Plan:

    TILES = {0: ("K", 0, 2), 1: ("O", -1, 0), 2: ("O", -1, 1), 3: ("O", -1, 2), 4: ("O", -1, 3),
             5: ("Q", 0, 2), 6: ("K", 0, 3), 7: ("Q", 0, 3),
             8: ("V", 1, 0), 9: ("V", 1, 1), 10: ("V", 1, 2), 11: ("V", 1, 3),
             12: ("K", 1, 0), 13: ("Q", 1, 0), 14: ("K", 1, 1), 15: ("Q", 1, 1)}

    def __init__(self):
        self.at = {}
        for block in range(START // HG, END // HG):
            kind, seq, n = self.TILES[block % BPS]
            seq += block // BPS
            if 0 <= seq < NB:
                self.at[block] = (kind, seq, n)

    def tile(self, block):
        return self.at.get(block)

    def count(self, kinds, block):
        return sum(1 for b, t in self.at.items() if b <= block and t[0] in kinds)

    def before(self, block):
        return max((b for b in self.at if b < block), default=None)

    def block_of(self, kind, seq, n):
        return next((b for b, t in self.at.items() if t == (kind, seq, n)), None)


PLAN = Plan()


def items_with(step):
    return min(step + 1, STEPS) + (max(0, (step - 3) // SPG) if step >= 3 else 0)


SPG = NC * HG


def items_with_recip(group):
    return items_with((group + 1) * SPG + 2) + 1


def by_vector(step):
    return step % HG == HG - 1


def copies_scalar(step):
    full, rest = divmod(step + 1, HG)
    return full * (HG - 1) + min(rest, HG - 1)


def copies_vector(step):
    return (step + 1) // HG


def xattn_program(nc, x, xT, cT, mask, WqT, WkT, WvT, WoT, bq, bk, bv, bo, ln_g, ln_b, out):
    with ExitStack() as ctx:
        def sb(name, shape, dt=FP32):
            return ctx.enter_context(nc.sbuf_tensor(name, shape, dt))

        def bank(name):
            return ctx.enter_context(nc.psum_tensor(name, [P, L], FP32))

        w_hi = {n: sb(f"w{n}_hi", [P, NK, H], FP32R) for n in "qkv"}
        w_lo = {n: sb(f"w{n}_lo", [P, NK, H], FP32R) for n in "qkv"}
        wo = sb("wo", [P, NK, H])
        c_hi, c_lo = sb("c_hi", [P, NK, L], FP32R), sb("c_lo", [P, NK, L], FP32R)
        x_hi, x_lo = sb("x_hi", [P, NK, L], FP32R), sb("x_lo", [P, NK, L], FP32R)
        raw = sb("raw", [P, NK, L])
        q_hi, q_lo = sb("q_hi", [P, L], FP32R), sb("q_lo", [P, L], FP32R)
        k_hi, k_lo = sb("k_hi", [P, L], FP32R), sb("k_lo", [P, L], FP32R)
        q_stack = sb("q_stack", [P, 2 * HG, L], FP32R)
        k_stack = sb("k_stack", [P, 2 * HG, L], FP32R)
        v = sb("v", [P, 2, NC, H])
        bias = sb("bias", [P, 2, NC, L], BF16)
        probs = sb("probs", [P, 2, L])
        probsT = sb("probsT", [P, 2, NC, HG, P])
        sums = sb("sums", [P, 2, SPG])
        recip = sb("recip", [P, SPG])
        recip_wide = sb("recip_wide", [P, SPG, D])
        recipT = sb("recipT", [P, L])
        ctxT = sb("ctxT", [P, NG, L])
        rows = sb("rows", [P, NC, L])
        negmax = sb("negmax", [P, 8])
        ident = sb("ident", [P, P])
        ident_bf = sb("ident_bf", [P, P], BF16)
        bq_s, bk_s, bv_s = sb("bq_s", [P, NG]), sb("bk_s", [P, NG]), sb("bv_s", [P, NG])
        bo_all = sb("bo_all", [P, H])
        g_all, b_all = sb("g_all", [P, H]), sb("b_all", [P, H])
        stats = sb("stats", [P, 2, 6])
        moments = sb("moments", [P, 2, 2])
        rstd = sb("rstd", [P, 2])
        eps_t, half_t = sb("eps_t", [P, 1]), sb("half_t", [P, 1])

        score_bank = [bank(f"score_bank{n}") for n in range(4)]
        trans_bank = [bank(f"trans_bank{n}") for n in range(2)]
        ctx_bank = bank("ctx_bank")
        proj_bank = bank("proj_bank")

        per_turn = {}

        def sem(name, turn=0):
            s = ctx.enter_context(nc.semaphore(name))
            per_turn[name] = turn
            return s, name

        blocks, groups = TURN // HG, TURN // SPG
        weights_loaded = [sem(f"weights_loaded{n}") for n in range(4)]
        consts_loaded = sem("consts_loaded")
        consts_made = sem("consts_made")
        start_chain = sem("start_chain")
        weights_split = sem("weights_split")
        wo_bv = sem("wo_bv")
        scores_ready = sem("scores_ready", TURN)
        transposed = sem("transposed", TURN + groups)
        ctx_summed = sem("ctx_summed", blocks)
        projected = sem("projected", blocks)
        probs_ready = sem("probs_ready", TURN)
        probsT_scalar = sem("probsT_scalar", TURN - blocks)
        recipT_ready = sem("recipT_ready", groups)
        hi_ready = sem("hi_ready", groups * 2)
        v_ready = sem("v_ready", SEQS_PER_TURN * NC)
        max_ready = sem("max_ready", TURN)
        probsT_vector = sem("probsT_vector", blocks)
        recip_small = sem("recip_small", groups)
        recip_ready = sem("recip_ready", groups)
        ctx_ready = sem("ctx_ready", groups)
        lo_ready = sem("lo_ready", groups * 2)
        row_sum = sem("row_sum", SEQS_PER_TURN * NC)
        row_stats = sem("row_stats", SEQS_PER_TURN * NC)
        stats_seen = sem("stats_seen")
        row_moments = sem("row_moments", SEQS_PER_TURN * NC)
        row_normed = sem("row_normed", SEQS_PER_TURN * NC)
        hi_split = sem("hi_split", SEQS_PER_TURN * NK * 2)
        bias_ready = sem("bias_ready", SEQS_PER_TURN * NC)
        rows_biased = sem("rows_biased", SEQS_PER_TURN * NC)
        eps_added = sem("eps_added", SEQS_PER_TURN * NC)
        rstd_ready = sem("rstd_ready", SEQS_PER_TURN * NC)
        row_scaled = sem("row_scaled", SEQS_PER_TURN * NC)
        row_done = sem("row_done", SEQS_PER_TURN * NC)
        lo_split = sem("lo_split", SEQS_PER_TURN * NK * 2)
        raw_loaded = [sem(f"raw_loaded{n}", SEQS_PER_TURN * 3 * FULL) for n in range(NK)]
        rows_loaded = [sem(f"rows_loaded{n}", SEQS_PER_TURN * FULL) for n in range(NC)]
        rows_stored = [sem(f"rows_stored{n}", SEQS_PER_TURN * FULL) for n in range(NC)]
        STACKED = 3 * HG * FULL
        q_stacked = [sem(f"q_stacked{n}", groups // 2 * STACKED) for n in range(2)]
        k_stacked = [sem(f"k_stacked{n}", groups // 2 * STACKED) for n in range(2)]

        def wait(eng, s, n, turn):
            if n <= 0:
                return
            sem_, name = s
            eng.wait_ge(sem_, n if turn is None else turn * per_turn[name] + n)

        def wait_all(eng, waits, turn):
            if turn is not None:
                waits = [(s, eng.to_reg(turn * per_turn[s[1]] + n)) for s, n in waits]
                turn = None
            for s, n in waits:
                if not isinstance(n, int) or n > 0:
                    eng.wait_ge(s[0], n)

        def walk(eng, body):
            for step in range(START, TURN):
                body(step, None)
            with eng.Fori(0, STEPS // TURN - 2) as turn:
                for step in range(TURN, 2 * TURN):
                    body(step, turn)
            for step in range(STEPS - TURN, END):
                body(step, None)

        def walk_sequences(eng, body):
            for seq in range(-1, SEQS_PER_TURN):
                body(seq, None)
            with eng.Fori(0, STEPS // TURN - 2) as turn:
                for seq in range(SEQS_PER_TURN, 2 * SEQS_PER_TURN):
                    body(seq, turn)
            for seq in range(NB - SEQS_PER_TURN, NB + 1):
                body(seq, None)

        def seq_of(seq, turn):
            return seq if turn is None else turn * SEQS_PER_TURN + seq

        def split_block(which, n, seq):
            first = {"c": 6 * HG + 3, "x": 8 * HG, "mask": 10 * HG}[which]
            return (seq - 1) * SPS + first + n

        block = ctx.enter_context(nc.Block())

        @block.sync
        def _(sp):
            for n, (w, dst) in enumerate(((WvT, v[:, 1]), (WkT, w_stage(probsT)),
                                          (WqT, ctxT[:, :, :]), (WoT, wo[:, :, :]))):
                sp.dma_start(dst, w.rearrange("(t p) n -> p t n", p=P)).then_inc(
                    weights_loaded[n][0], FULL)
            for dst, src in ((bq_s, bq), (bk_s, bk), (bv_s, bv), (bo_all, bo), (g_all, ln_g),
                             (b_all, ln_b)):
                sp.dma_start(dst[:, :], src).then_inc(consts_loaded[0], FULL)

            def load_raw(which, src, seq, turn):
                use = {"c": 0, "x": 1, "mask": 2}[which]
                for t in range(NK):
                    if which == "c":
                        wait(sp, bias_ready, NC * seq - NC + t + 1 if seq else 0, turn)
                    else:
                        wait(sp, lo_split, 2 * NK * seq + (use - 1) * NK + t + 1, turn)
                    dst = raw[:, t] if which != "mask" else raw[:, t].bitcast(INT32)
                    sp.dma_start(dst, src[bass.ds(seq_of(seq, turn), 1), t * P:(t + 1) * P, :]
                                 .rearrange("a p n -> (a p) n")).then_inc(raw_loaded[t][0], FULL)

            def stack(kind, seq, group, turn):
                n = seq * NG + group
                at = PLAN.block_of(kind, seq, group)
                wait_all(sp, ((hi_ready, PLAN.count("QK", at)), (lo_ready, PLAN.count("QK", at)),
                              (scores_ready, (n - 1) * SPG)), turn)
                hi, lo, dst, done = ((q_hi, q_lo, q_stack, q_stacked) if kind == "Q"
                                     else (k_hi, k_lo, k_stack, k_stacked))
                order = (hi, lo, hi) if kind == "Q" else (hi, hi, lo)
                for h in range(HG):
                    for part, src in enumerate(order):
                        sp.dma_start(
                            dst[part * D:(part + 1) * D, (n % 2) * HG + h, :].bitcast(FP32),
                            src[h * D:(h + 1) * D, :].bitcast(FP32)).then_inc(
                            done[n % 2][0], FULL)

            def load_rows(seq, turn):
                for j in range(NC):
                    wait(sp, rows_stored[j], FULL * seq, turn)
                    sp.dma_start(rows[:, j], x[bass.ds(seq_of(seq, turn), 1), j * P:(j + 1) * P, :]
                                 .rearrange("a p n -> (a p) n")).then_inc(rows_loaded[j][0], FULL)

            def store_row(seq, j, turn):
                wait(sp, row_done, seq * NC + j + 1, turn)
                sp.dma_start(out[bass.ds(seq_of(seq, turn), 1), j * P:(j + 1) * P, :]
                             .rearrange("a p n -> (a p) n"), rows[:, j]).then_inc(
                    rows_stored[j][0], FULL)

            def sequence(seq, turn):
                here, before, after = 0 <= seq < NB, seq >= 1, seq + 1 < NB
                if before:
                    load_rows(seq - 1, turn)
                if after:
                    load_raw("c", cT, seq + 1, turn)
                if here:
                    stack("K", seq, 2, turn)
                if before:
                    for j in range(NC - 1):
                        store_row(seq - 1, j, turn)
                if here:
                    stack("Q", seq, 2, turn)
                if before:
                    store_row(seq - 1, NC - 1, turn)
                if here:
                    stack("K", seq, 3, turn)
                if after:
                    load_raw("x", xT, seq + 1, turn)
                if here:
                    stack("Q", seq, 3, turn)
                if after:
                    load_raw("mask", mask, seq + 1, turn)
                    for group in range(2):
                        stack("K", seq + 1, group, turn)
                        stack("Q", seq + 1, group, turn)

            walk_sequences(sp, sequence)
            for j in range(NC):
                sp.wait_ge(rows_stored[j][0], FULL * NB)

        @block.gpsimd
        def _(pool):
            nc.gpsimd.memset(ident[:, :], 0.0).then_inc(consts_made[0], 1)
            nc.gpsimd.memset(eps_t[:, :], EPS).then_inc(consts_made[0], 1)
            nc.gpsimd.memset(half_t[:, :], -0.5).then_inc(consts_made[0], 1)
            pool.wait_ge(consts_made[0], 3)
            nc.gpsimd.affine_select(out=ident[:, :], in_=ident[:, :], compare_op=ALU.not_equal,
                                    fill=1.0, base=0, pattern=[[-1, P]],
                                    channel_multiplier=1).then_inc(consts_made[0], 1)
            pool.wait_ge(consts_made[0], 4)
            nc.gpsimd.tensor_copy(ident_bf[:, :], ident[:, :]).then_inc(consts_made[0], 1)
            pool.wait_ge(start_chain[0], 4)

            def sequence(seq, turn):
                if seq >= 1:
                    for j in range(NC):
                        wait(pool, rows_loaded[j], FULL * seq, turn)
                        nc.gpsimd.tensor_tensor(rows[:, j], rows[:, j], bo_all[:, :],
                                                ALU.add).then_inc(rows_biased[0], 1)
                    for j in range(NC):
                        n = (seq - 1) * NC + j
                        wait(pool, row_moments, n + 1, turn)
                        wait(pool, row_normed, n - 1, turn)
                        nc.gpsimd.tensor_tensor(rstd[:, j % 2:j % 2 + 1], moments[:, j % 2, 1:2],
                                                eps_t[:, :], ALU.add).then_inc(eps_added[0], 1)
                        wait(pool, eps_added, n + 1, turn)
                        nc.gpsimd.tensor_tensor(rstd[:, j % 2:j % 2 + 1], rstd[:, j % 2:j % 2 + 1],
                                                half_t[:, :], ALU.pow).then_inc(rstd_ready[0], 1)
                        wait(pool, row_normed, n + 1, turn)
                        nc.gpsimd.tensor_tensor(rows[:, j], rows[:, j], g_all[:, :],
                                                ALU.mult).then_inc(row_scaled[0], 1)
                        wait(pool, row_scaled, n + 1, turn)
                        nc.gpsimd.tensor_tensor(rows[:, j], rows[:, j], b_all[:, :],
                                                ALU.add).then_inc(row_done[0], 1)
                if seq + 1 < NB:
                    for use, (hi, lo) in enumerate(((c_hi, c_lo), (x_hi, x_lo))):
                        for t in range(NK):
                            n = 2 * NK * (seq + 1) + use * NK + t
                            wait(pool, hi_split, n + 1, turn)
                            nc.gpsimd.tensor_tensor(lo[:, t], raw[:, t], hi[:, t].bitcast(FP32),
                                                    ALU.subtract).then_inc(lo_split[0], 1)

            walk_sequences(pool, sequence)

        @block.scalar
        def _(act):
            def step_(step, turn):
                blk, head = divmod(step, HG)
                tile = PLAN.tile(blk)
                if head == HG - 1 and tile and tile[0] != "O":
                    kind, seq, n = tile
                    wait(act, projected, PLAN.count("QKVO", blk), turn)
                    if kind == "V":
                        wait(act, ctx_summed, (seq - 1) * BPS, turn)
                        nc.scalar.copy(v[:, seq % 2, n], proj_bank[:, :]).then_inc(v_ready[0], 1)
                    else:
                        hi, b_, done = ((q_hi, bq_s, q_stacked) if kind == "Q"
                                        else (k_hi, bk_s, k_stacked))
                        g = seq * NG + n - 1
                        wait(act, done[g % 2], (g // 2 + 1) * STACKED, turn)
                        nc.scalar.activation(hi[:, :], proj_bank[:, :], ACT.Identity,
                                             bias=b_[:, n:n + 1]).then_inc(hi_ready[0], 1)
                s = step + 1
                if 0 <= s < STEPS:
                    wait(act, max_ready, s + 1, turn)
                    wait(act, transposed, items_with(s - 2) if s >= 2 else 0, turn)
                    g, at = divmod(s, SPG)
                    if at == 0:
                        wait(act, recip_small, g - 1, turn)
                    nc.scalar.activation(probs[:, s % 2], score_bank[s % 4][:, :], ACT.Exp,
                                         bias=negmax[:, s % 8:s % 8 + 1],
                                         accum_out=sums[:, g % 2, at:at + 1]).then_inc(
                        probs_ready[0], 1)
                if 0 <= step < STEPS and not by_vector(step):
                    copy_transposed(act, step, turn)
                if step % SPG == 2 and step > SPG and step // SPG <= NB * NG:
                    g = step // SPG - 1
                    wait(act, transposed, items_with_recip(g), turn)
                    wait(act, ctx_ready, g, turn)
                    nc.scalar.copy(recipT[:, :], trans_bank[(items_with_recip(g) - 1) % 2][:, :]
                                   ).then_inc(recipT_ready[0], 1)

            def copy_transposed(eng, step, turn):
                blk, head = divmod(step, HG)
                wait(act, transposed, items_with(step), turn)
                wait(act, ctx_summed, blk - 1, turn)
                nc.scalar.copy(probsT[:, blk % 2, :, head, :],
                               trans_bank[(items_with(step) - 1) % 2][:, :].rearrange(
                                   "p (c q) -> p c q", c=NC)).then_inc(probsT_scalar[0], 1)

            act.wait_ge(start_chain[0], 4)
            walk(act, step_)

        @block.vector
        def _(dve):
            dve.wait_ge(weights_loaded[0][0], FULL)
            split_weight(nc, dve, w_hi["v"], w_lo["v"], v[:, 1], weights_split, 1)
            dve.wait_ge(weights_loaded[1][0], FULL)
            split_weight(nc, dve, w_hi["k"], w_lo["k"], w_stage(probsT), weights_split, 3)
            dve.wait_ge(weights_loaded[2][0], FULL)
            nc.vector.tensor_scalar(ctxT[:, :, :], ctxT[:, :, :], SCALE, None,
                                    ALU.mult).then_inc(start_chain[0], 1)
            dve.wait_ge(consts_loaded[0], 6 * FULL)
            nc.vector.tensor_scalar(bq_s[:, :], bq_s[:, :], SCALE, None,
                                    ALU.mult).then_inc(start_chain[0], 1)
            dve.wait_ge(start_chain[0], 2)
            split_weight(nc, dve, w_hi["q"], w_lo["q"], ctxT[:, :, :], weights_split, 5)
            nc.vector.tensor_copy(recip_wide[:, :, :].rearrange("p (g a) d -> p g (a d)", g=NG),
                                  bv_s[:, :].unsqueeze(2).to_broadcast([P, NG, P])).then_inc(
                start_chain[0], 1)
            dve.wait_ge(wo_bv[0], 1)
            nc.vector.tensor_tensor(bo_all[:, :], proj_bank[:, :], bo_all[:, :],
                                    ALU.add).then_inc(start_chain[0], 1)

            def step_(step, turn):
                blk, head = divmod(step, HG)
                seq = blk // BPS
                tile, last = PLAN.tile(blk), PLAN.tile(blk - 1)
                if step % SPG == 0 and 1 <= step // SPG <= NB * NG:
                    g = step // SPG - 1
                    wait(dve, probs_ready, (g + 1) * SPG, turn)
                    wait(dve, recip_ready, g, turn)
                    nc.vector.reciprocal(recip[:, :], sums[:, g % 2]).then_inc(recip_small[0], 1)
                s = step + 2
                if 0 <= s < STEPS:
                    wait(dve, scores_ready, s + 1, turn)
                    wait(dve, probs_ready, s - 7, turn)
                    nc.vector.tensor_reduce(negmax[:, s % 8:s % 8 + 1], score_bank[s % 4][:, :],
                                            AX.X, ALU.max, negate=True).then_inc(max_ready[0], 1)
                if step % SPG == 0 and 1 <= step // SPG <= NB * NG:
                    wait(dve, recip_small, g + 1, turn)
                    wait(dve, transposed, items_with_recip(g - 1) if g else 0, turn)
                    nc.vector.tensor_copy(recip_wide[:, :, :], recip[:, :].unsqueeze(2)
                                          .to_broadcast([P, SPG, D])).then_inc(recip_ready[0], 1)
                if step % SPG == HG and 1 <= step // SPG <= NB * NG:
                    g = step // SPG - 1
                    wait(dve, ctx_summed, (g + 1) * NC, turn)
                    wait(dve, recipT_ready, g + 1, turn)
                    if g % NG == 0:
                        wait(dve, projected, PLAN.count("QKVO", blk - 1), turn)
                    nc.vector.tensor_tensor(ctxT[:, g % NG], ctx_bank[:, :], recipT[:, :],
                                            ALU.mult).then_inc(ctx_ready[0], 1)
                if head == HG - 1 and tile and tile[0] in "QK":
                    kind, seq_t, n = tile
                    hi, lo, b_, done = ((q_hi, q_lo, bq_s, q_stacked) if kind == "Q"
                                        else (k_hi, k_lo, bk_s, k_stacked))
                    g = seq_t * NG + n - 1
                    wait(dve, hi_ready, PLAN.count("QK", blk), turn)
                    wait(dve, done[g % 2], (g // 2 + 1) * STACKED, turn)
                    nc.vector.scalar_tensor_tensor(
                        out=lo[:, :], in0=proj_bank[:, :], scalar=b_[:, n:n + 1],
                        in1=hi[:, :].bitcast(FP32), op0=ALU.add,
                        op1=ALU.subtract).then_inc(lo_ready[0], 1)
                if head == HG - 1 and tile and tile[0] == "O":
                    n = tile[1] * NC + tile[2]
                    wait(dve, projected, PLAN.count("QKVO", blk), turn)
                    wait(dve, rows_biased, n + 1, turn)
                    nc.vector.tensor_tensor(rows[:, tile[2]], proj_bank[:, :], rows[:, tile[2]],
                                            ALU.add).then_inc(row_sum[0], 1)
                if 0 <= step < STEPS and by_vector(step):
                    wait(dve, transposed, items_with(step), turn)
                    wait(dve, ctx_summed, blk - 1, turn)
                    nc.vector.tensor_copy(probsT[:, blk % 2, :, head, :],
                                          trans_bank[(items_with(step) - 1) % 2][:, :].rearrange(
                                              "p (c q) -> p c q", c=NC)).then_inc(
                        probsT_vector[0], 1)
                if last and last[0] == "O":
                    j = last[2]
                    n = last[1] * NC + j
                    if head == 0:
                        wait(dve, row_sum, n + 1, turn)
                        wait(dve, row_moments, n - 1, turn)
                        nc.vector.bn_stats(stats[:, j % 2], rows[:, j]).then_inc(row_stats[0], 1)
                    if head == 1:
                        wait(dve, row_stats, n + 1, turn)
                        wait(dve, row_normed, n - 1, turn)
                        dve.sem_inc(stats_seen[0], 1)
                        nc.vector.bn_aggr(moments[:, j % 2], stats[:, j % 2]).then_inc(
                            row_moments[0], 1)
                    if head == 3:
                        wait(dve, row_moments, n + 1, turn)
                        wait(dve, rstd_ready, n + 1, turn)
                        nc.vector.tensor_scalar(rows[:, j], rows[:, j], moments[:, j % 2, 0:1],
                                                rstd[:, j % 2:j % 2 + 1], ALU.subtract,
                                                ALU.mult).then_inc(row_normed[0], 1)
                for which, hi in (("c", c_hi), ("x", x_hi), ("mask", None)):
                    for t in range(NK):
                        for to in (seq, seq + 1):
                            if not 0 <= to < NB or split_block(which, t, to) != step:
                                continue
                            use = {"c": 0, "x": 1, "mask": 2}[which]
                            wait(dve, raw_loaded[t], FULL * (3 * to + use + 1), turn)
                            if which == "mask":
                                wait(dve, scores_ready, (to - 1) * SPS, turn)
                                nc.vector.tensor_scalar(
                                    bias[:, to % 2, t], raw[:, t].bitcast(INT32), 0.0, MASKED,
                                    ALU.is_equal, ALU.mult).then_inc(bias_ready[0], 1)
                            else:
                                wait(dve, projected, PLAN.count("QKVO", PLAN.block_of(
                                    "K" if which == "c" else "Q", to - 1, NG - 1)) if to else 0,
                                    turn)
                                nc.vector.tensor_copy(hi[:, t], raw[:, t]).then_inc(
                                    hi_split[0], 1)

            walk(dve, step_)

        @block.tensor
        def _(pe):
            pe.wait_ge(consts_made[0], 5)
            pe.wait_ge(weights_loaded[3][0], FULL)
            pe.wait_ge(start_chain[0], 3)
            for t in range(NK):
                last = nc.tensor.matmul(proj_bank[:, :], recip_wide[:, t * 4:(t + 1) * 4, :]
                                        .rearrange("p a d -> p (a d)"), wo[:, t],
                                        start=t == 0, stop=t == NK - 1)
            last.then_inc(wo_bv[0], 1)
            pe.wait_ge(start_chain[0], 4)
            pe.wait_ge(weights_split[0], 6)

            def bank_is_free(item, turn):
                if item < 3:
                    return
                for s in copied_before[item - 2]:
                    wait(pe, s[0], s[1], turn)

            def scores(s, turn):
                g, at = divmod(s, SPG)
                c, h = divmod(at, HG)
                slot = (g % 2) * HG + h
                wait(pe, probs_ready, s - 3, turn)
                if at == 0:
                    wait(pe, q_stacked[g % 2], (g // 2 + 1) * STACKED, turn)
                    wait(pe, k_stacked[g % 2], (g // 2 + 1) * STACKED, turn)
                    if g % NG == 0:
                        wait(pe, bias_ready, (g // NG + 1) * NC, turn)
                out_ = score_bank[s % 4][:, :]
                nc.tensor.matmul(out_, q_stack[0:3 * D, slot, c * P:(c + 1) * P],
                                 k_stack[0:3 * D, slot, :], start=True, stop=False)
                nc.tensor.matmul(out_, ident_bf[:, :], bias[:, (g // NG) % 2, c], start=False,
                                 stop=True).then_inc(scores_ready[0], 1)

            def projection(blk, head, turn):
                tile = PLAN.tile(blk)
                if not tile or head == HG - 1:
                    return
                kind, seq, n = tile
                if head == 0:
                    b = PLAN.before(blk)
                    if b is not None:
                        k = PLAN.tile(b)[0]
                        s = {"Q": lo_ready, "K": lo_ready, "V": v_ready, "O": row_sum}[k]
                        wait(pe, s, PLAN.count("QK" if k in "QK" else k, b), turn)
                cols = slice(n * P, (n + 1) * P)
                if kind == "O":
                    if head == 0:
                        wait(pe, ctx_ready, (seq + 1) * NG, turn)
                    parts = [(ctxT[:, t, cols], wo[:, t], t) for t in range(NK)]
                    share = ((0, 2), (2, 3), (3, 4))[head]
                else:
                    hi, lo = (x_hi, x_lo) if kind == "Q" else (c_hi, c_lo)
                    wh, wl = w_hi[kind.lower()], w_lo[kind.lower()]
                    parts = []
                    for t in range(NK):
                        a, b_, u, w = ((hi, lo, wh, wl) if kind == "V" else (wh, wl, hi, lo))
                        parts += [(a[:, t, cols], u[:, t], t), (b_[:, t, cols], u[:, t], t),
                                  (a[:, t, cols], w[:, t], t)]
                    share = (4 * head, 4 * head + 4)
                for m in range(*share):
                    a, u, t = parts[m]
                    if kind != "O" and m % 3 == 0:
                        at = 2 * NK * seq + (NK if kind == "Q" else 0) + t + 1
                        if (kind, n) in (("V", 0), ("Q", 0)):
                            wait(pe, lo_split, at, turn)
                    last = nc.tensor.matmul(proj_bank[:, :], a, u, start=m == 0,
                                            stop=m == len(parts) - 1)
                if share[1] == len(parts):
                    last.then_inc(projected[0], 1)

            def transposes(step, turn):
                item = items_with(step)
                wait(pe, probs_ready, step + 1, turn)
                bank_is_free(item, turn)
                for c in range(NC):
                    last = nc.tensor.transpose(trans_bank[(item - 1) % 2][:, c * P:(c + 1) * P],
                                               probs[:, step % 2, c * P:(c + 1) * P], ident[:, :])
                last.then_inc(transposed[0], 1)

            def recip_transposes(g, turn):
                item = items_with_recip(g)
                wait(pe, recip_ready, g + 1, turn)
                bank_is_free(item, turn)
                for c in range(NC):
                    last = nc.tensor.transpose(
                        trans_bank[(item - 1) % 2][:, c * P:(c + 1) * P],
                        recip_wide[:, c * HG:(c + 1) * HG, :].rearrange("p a d -> p (a d)"),
                        ident[:, :])
                last.then_inc(transposed[0], 1)

            def context(blk, kc, turn):
                g, c = divmod(blk, NC)
                if kc == 0:
                    wait(pe, probsT_scalar, copies_scalar(blk * HG + HG - 1), turn)
                    wait(pe, probsT_vector, copies_vector(blk * HG + HG - 1), turn)
                    if c == 0:
                        wait(pe, ctx_ready, g, turn)
                        if g % NG == 0:
                            wait(pe, v_ready, (g // NG + 1) * NC, turn)
                for h in range(HG):
                    col = (g % NG * HG + h) * D
                    last = nc.tensor.matmul(
                        ctx_bank[h * D:(h + 1) * D, c * P:(c + 1) * P],
                        v[:, (g // NG) % 2, kc, col:col + D], probsT[:, blk % 2, kc, h, :],
                        start=kc == 0, stop=kc == NC - 1)
                if kc == NC - 1:
                    last.then_inc(ctx_summed[0], 1)

            copied_before = {}
            for s in range(STEPS):
                copied_before[items_with(s)] = [(probsT_vector, copies_vector(s)) if by_vector(s)
                                                else (probsT_scalar, copies_scalar(s))]
            for g in range(NB * NG):
                copied_before[items_with_recip(g)] = [(recipT_ready, g + 1)]

            def step_(step, turn):
                blk, head = divmod(step, HG)
                if 0 <= step < STEPS:
                    transposes(step, turn)
                if 0 <= step + LEAD < STEPS:
                    scores(step + LEAD, turn)
                projection(blk, head, turn)
                if 1 <= blk <= STEPS // HG:
                    for kc in CHUNKS_AT[head]:
                        context(blk - 1, kc, turn)
                if step % SPG == 2 and step > SPG and step // SPG <= NB * NG:
                    recip_transposes(step // SPG - 1, turn)

            walk(pe, step_)


def w_stage(probsT):
    return probsT[:, :, :, :, :].rearrange("p a c h q -> p (a c h q)")[:, 0:NK * H].rearrange(
        "p (t n) -> p t n", t=NK)


def split_weight(nc, dve, hi, lo, src, done, count):
    nc.vector.tensor_copy(hi[:, :, :], src).then_inc(done[0], 1)
    dve.wait_ge(done[0], count)
    nc.vector.tensor_tensor(lo[:, :, :], src, hi[:, :, :].bitcast(FP32),
                            ALU.subtract).then_inc(done[0], 1)


def kernel(x, ctx_1024, mask_BxSxS2_ik1, L0_xattn_Wq, L0_xattn_bq, L0_xattn_Wk, L0_xattn_bk,
           L0_xattn_Wv, L0_xattn_bv, L0_xattn_Wo, L0_xattn_bo, L0_xattn_ln_g, L0_xattn_ln_b):
    import numpy as np
    import concourse.bacc as bacc
    from concourse.bass_utils import run_bass_kernel_spmd

    def a(t):
        return np.asarray(t)

    def columns(t):
        return np.ascontiguousarray(a(t).reshape(NG, P).T)

    def everywhere(t):
        return np.ascontiguousarray(np.broadcast_to(a(t), (P, H)))

    ins = {
        "x_dram": np.ascontiguousarray(a(x)),
        "xT_dram": np.ascontiguousarray(a(x).transpose(0, 2, 1)),
        "cT_dram": np.ascontiguousarray(a(ctx_1024).transpose(0, 2, 1)),
        "mask_dram": np.ascontiguousarray(a(mask_BxSxS2_ik1)),
        "WqT_dram": np.ascontiguousarray(a(L0_xattn_Wq).T),
        "WkT_dram": np.ascontiguousarray(a(L0_xattn_Wk).T),
        "WvT_dram": np.ascontiguousarray(a(L0_xattn_Wv).T),
        "WoT_dram": np.ascontiguousarray(a(L0_xattn_Wo).T),
        "bq_dram": columns(L0_xattn_bq),
        "bk_dram": columns(L0_xattn_bk),
        "bv_dram": columns(L0_xattn_bv),
        "bo_dram": everywhere(L0_xattn_bo),
        "ln_g_dram": everywhere(L0_xattn_ln_g),
        "ln_b_dram": everywhere(L0_xattn_ln_b),
    }
    nc = bacc.Bacc("TRN2", target_bir_lowering=False, num_devices=1)
    aps = [nc.dram_tensor(n, t.shape, mybir.dt.from_np(t.dtype), kind="ExternalInput").ap()
           for n, t in ins.items()]
    aps.append(nc.dram_tensor("out_dram", (NB, L, H), FP32, kind="ExternalOutput").ap())
    xattn_program(nc, *aps)
    r = run_bass_kernel_spmd(nc, [ins], core_ids=[0])
    return r.results[0]["out_dram"]
```
